# Optimizing a Trainium2 kernel written in Bass

```python
import numpy as np
import jax
import jax.numpy as jnp

def _softmax(x, axis=-1):
    return jax.nn.softmax(x, axis=axis)

def _gelu(x):
    return jax.nn.gelu(x, approximate=True)

def _silu(x):
    return jax.nn.silu(x)

def _sigmoid(x):
    return jax.nn.sigmoid(x)

def _layernorm(x, axis=-1, eps=1e-05):
    m = jnp.mean(x, axis=axis, keepdims=True)
    v = jnp.var(x, axis=axis, keepdims=True)
    return (x - m) / jnp.sqrt(v + eps)

def _scatter_add(tgt, idx, src, axis=0):
    return tgt.at[idx].add(src)

def _segment_sum(src, seg, n):
    return jax.ops.segment_sum(src, seg, n)
kernel_name = 'mk_gnn_ffn_d1_gnn_r8_0a1834'

def setup_inputs(seed: int=0):
    np.random.seed(seed)
    _w = jnp.asarray

    def _rec_inputs():
        import jax
        import jax.numpy as jnp
        _gk = jax.random.key(seed)
        x = -0.0002117 + 1 * jax.random.normal(jax.random.fold_in(_gk, 1), (6250, 256), jnp.float32)
        src = jax.random.randint(jax.random.fold_in(_gk, 2), (200000,), 0, 6250, jnp.int32)
        dst = jax.random.randint(jax.random.fold_in(_gk, 3), (200000,), 0, 6250, jnp.int32)
        _o = jnp.argsort(dst, stable=True)
        src = src[_o]
        dst = dst[_o]
        edge_weight = jax.random.uniform(jax.random.fold_in(_gk, 12), (200000,), jnp.float32, 0.0, 0.03125)
        return (x, src, dst, edge_weight)
    x, src, dst, edge_weight = _rec_inputs()

    def _L0_gnn_setup():
        import jax, jax.numpy as jnp
        import numpy as np
        N_NODES = 12500
        N_EDGES = 400000
        D_IN = 256
        N_BLOCKS = 4
        D_OUT = 256

        def _spmm(edge_src, edge_dst, edge_weight, feats, n_nodes):
            msgs = edge_weight[:, None] * feats[edge_src]
            return jax.ops.segment_sum(msgs, edge_dst, num_segments=n_nodes)
        key = jax.random.key(seed)
        ks = jax.random.split(key, 6)
        x = jax.random.normal(ks[0], (N_NODES, D_IN), dtype=jnp.float32)
        edge_src = jax.random.randint(ks[1], (N_EDGES,), 0, N_NODES, dtype=jnp.int32)
        edge_dst = jax.random.randint(ks[2], (N_EDGES,), 0, N_NODES, dtype=jnp.int32)
        edge_weight = jax.random.uniform(ks[3], (N_EDGES,), dtype=jnp.float32) / 32.0
        stdv_w = 1.0 / np.sqrt(D_OUT)
        shared_weight = jax.random.uniform(ks[4], (D_IN * N_BLOCKS, D_OUT), minval=-stdv_w, maxval=stdv_w, dtype=jnp.float32)
        stdv_b = 1.0 / np.sqrt(D_OUT)
        output_bias = jax.random.uniform(ks[5], (D_OUT,), minval=-stdv_b, maxval=stdv_b, dtype=jnp.float32)
        return {'x': x, 'edge_src': edge_src, 'edge_dst': edge_dst, 'edge_weight': edge_weight, 'shared_weight': shared_weight, 'output_bias': output_bias}
    _L0_gnn_all = _L0_gnn_setup()
    _L0_gnn_in = {k: v for k, v in _L0_gnn_all.items() if k in ('shared_weight', 'output_bias')}
    del _L0_gnn_all

    def _L0_ffn_setup():
        import jax, jax.numpy as jnp
        import numpy as np
        B, S, D, E, H, K = (4, 512, 256, 8, 512, 2)
        key = jax.random.key(seed)
        ks = jax.random.split(key, 6)
        x = jax.random.normal(ks[0], (B, S, D), jnp.float32)
        Wg = jax.random.normal(ks[1], (D, E), jnp.float32) * 0.02
        bg = jnp.zeros((E,), jnp.float32)
        W1 = jax.random.normal(ks[2], (E, D, H), jnp.float32) * 0.02
        b1 = jnp.zeros((E, H), jnp.float32)
        W2 = jax.random.normal(ks[3], (E, H, D), jnp.float32) * 0.02
        b2 = jnp.zeros((E, D), jnp.float32)
        return {'x': x, 'Wg': Wg, 'bg': bg, 'W1': W1, 'b1': b1, 'W2': W2, 'b2': b2}
    _L0_ffn_all = _L0_ffn_setup()
    _L0_ffn_in = {k: v for k, v in _L0_ffn_all.items() if k in ('Wg', 'bg', 'W1', 'b1', 'W2', 'b2')}
    del _L0_ffn_all
    return {'x': x, 'src': src, 'dst': dst, 'edge_weight': edge_weight, 'L0_gnn_shared_weight': _L0_gnn_in['shared_weight'], 'L0_gnn_output_bias': _L0_gnn_in['output_bias'], 'L0_ffn_Wg': _L0_ffn_in['Wg'], 'L0_ffn_bg': _L0_ffn_in['bg'], 'L0_ffn_W1': _L0_ffn_in['W1'], 'L0_ffn_b1': _L0_ffn_in['b1'], 'L0_ffn_W2': _L0_ffn_in['W2'], 'L0_ffn_b2': _L0_ffn_in['b2']}

def reference(x, src, dst, edge_weight, L0_gnn_shared_weight, L0_gnn_output_bias, L0_ffn_Wg, L0_ffn_bg, L0_ffn_W1, L0_ffn_b1, L0_ffn_W2, L0_ffn_b2):
    import jax
    import jax.numpy as jnp

    def _L0_gnn_ref(x, edge_src, edge_dst, edge_weight, shared_weight, output_bias):
        import jax, jax.numpy as jnp
        import numpy as np
        N_NODES = 12500
        N_EDGES = 400000
        D_IN = 256
        N_BLOCKS = 4
        D_OUT = 256

        def _spmm(edge_src, edge_dst, edge_weight, feats, n_nodes):
            msgs = edge_weight[:, None] * feats[edge_src]
            return jax.ops.segment_sum(msgs, edge_dst, num_segments=n_nodes)
        n_nodes, d_in = x.shape
        n_blocks = shared_weight.shape[0] // d_in
        feats = [x]
        cur = x
        for _ in range(n_blocks - 1):
            cur = _spmm(edge_src, edge_dst, edge_weight, cur, n_nodes)
            feats.append(cur)
        concat = jnp.concatenate(feats, axis=1)
        return concat @ shared_weight + output_bias

    def _L0_ffn_ref(x, Wg, bg, W1, b1, W2, b2):
        import jax, jax.numpy as jnp
        import numpy as np
        B, S, D, E, H, K = (4, 512, 256, 8, 512, 2)
        Bv, Sv, Dv = x.shape
        gate_scores = x @ Wg + bg
        _, idx = jax.lax.top_k(gate_scores, K)
        mask = jax.nn.one_hot(idx, E, dtype=x.dtype).sum(axis=-2)
        xf = x.reshape(-1, Dv)
        mf = mask.reshape(-1, E)
        h = jax.nn.gelu(jnp.einsum('td,edh->teh', xf, W1) + b1[None], approximate=False)
        y = jnp.einsum('teh,ehd->ted', h, W2) + b2[None]
        out = jnp.einsum('ted,te->td', y, mf)
        return out.reshape(Bv, Sv, Dv)
    x = x + _L0_gnn_ref(_layernorm(x, axis=-1), src, dst, edge_weight, L0_gnn_shared_weight, L0_gnn_output_bias)
    x = x + _L0_ffn_ref(_layernorm(x, axis=-1)[None], L0_ffn_Wg, L0_ffn_bg, L0_ffn_W1, L0_ffn_b1, L0_ffn_W2, L0_ffn_b2)[0]
    return x

_drawn_inputs = setup_inputs


def setup_inputs(seed=0):
    import zlib

    import numpy as np

    out = dict(_drawn_inputs(seed))
    spreads = {'L0_ffn_bg': (0.0, 0.1), 'L0_ffn_b1': (0.0, 0.1), 'L0_ffn_b2': (0.0, 0.1)}
    factors = {}
    for name, (base, spread) in spreads.items():
        noise = np.random.default_rng([zlib.crc32(name.encode()), seed]).standard_normal(out[name].shape)
        drawn = base * np.exp(spread * noise) if base else spread * noise
        out[name] = jnp.asarray(drawn.astype(out[name].dtype))
    for name, factor in factors.items():
        out[name] = (out[name] * factor).astype(out[name].dtype)
    return out
```

```python
import numpy as np
import concourse.bass as bass
from concourse import mybir
from contextlib import ExitStack


def gnn_ffn_kernel(nc, x, src, dst, edge_weight, gnn_w, gnn_b, wg, bg, w1, b1, w2, b2, out):
    f32 = mybir.dt.float32
    i32 = mybir.dt.int32
    ALU = mybir.AluOpType
    ACT = mybir.ActivationFunctionType
    AX = mybir.AxisListType
    ds = bass.ds

    P = 128
    N, D = x.shape
    E = src.shape[0]
    NX, H = w1.shape[0], w1.shape[2]
    HOPS = gnn_w.shape[0] // D - 1
    TOPK = 2
    KD = D // P
    KH = H // P
    NT = -(-N // P)
    TAIL = N - (NT - 1) * P
    G = 7
    NG = NT // G
    assert NG * G == NT and KD == 2 and HOPS == 3
    ET = -(-E // P)
    U = 8
    IT = -(-(ET + NT - 1) // U)
    CH = -(-IT * U // P)
    NP = CH * P
    EFULL = E // P
    EREST = E - EFULL * P
    assert EREST > 0 and IT % 2 == 0
    FT = -(-(TOPK * N + NX * (P - 1)) // P)
    FT += FT % 2
    FROWS = FT * P
    DUMMY = TOPK * P
    EPS = 1e-5
    FAR = float(NT * P - 1)

    edges_d = nc.dram_tensor("edge_rows", (NP, 3 * P), i32, kind="Internal").ap()
    pairwin_d = nc.dram_tensor("pair_window", (NP,), i32, kind="Internal").ap()
    table_d = [nc.dram_tensor(f"hop_table_{h}", (NT * P, D), f32, kind="Internal").ap() for h in range(HOPS)]
    xe_d = nc.dram_tensor("expert_rows", (FROWS + P * TOPK, D), f32, kind="Internal").ap()
    ye_d = nc.dram_tensor("expert_out", (FROWS + P * TOPK, D), f32, kind="Internal").ap()

    ctx = ExitStack()
    with ctx:
        def sb(name, shape, dt=f32):
            return ctx.enter_context(nc.sbuf_tensor(name, shape, dt))

        def sem(name):
            return ctx.enter_context(nc.semaphore(name))

        acc0 = sb("acc0", [P, NT, D])
        acc1 = sb("acc1", [P, NT * D])
        acc2 = sb("acc2", [P, NT * D])
        accs = [acc1[:, :].rearrange("p (n d) -> p n d", d=D), acc2[:, :].rearrange("p (n d) -> p n d", d=D), acc0]
        stage = acc1[:, 0:CH * 3 * P].bitcast(i32).rearrange("p (c k) -> p c k", c=CH)
        stagef = acc2[:, 0:CH * 3 * P].rearrange("p (c k) -> p c k", c=CH)
        w1_sb = acc1[:, 0:KD * NX * H].rearrange("p (k m) -> p k m", k=KD)
        b1_sb = acc1[:, KD * NX * H:KD * NX * H + NX * H]
        w2_sb = acc2[:, 0:KH * NX * D].rearrange("p (k m) -> p k m", k=KH)
        b2_sb = acc2[:, KH * NX * D:KH * NX * D + NX * D]

        tables = sb("tables", [P, 3 * NP])
        src_t = tables[:, 0:NP].bitcast(i32)
        rel_t = tables[:, NP:2 * NP]
        wgt_t = tables[:, 2 * NP:3 * NP]

        work = sb("work", [P, 7680])
        wlin = work[:, 0:KD * 4 * D].rearrange("p (k m) -> p k m", k=KD)
        xn = work[:, 2048:2048 + G * D].rearrange("p (g d) -> p g d", g=G)
        xnT = work[:, 3840:3840 + G * D].rearrange("p (g k t) -> p g k t", g=G, k=KD)
        t3 = work[:, 5632:5632 + G * D].rearrange("p (g d) -> p g d", g=G)
        rows = work[:, 0:U * D].rearrange("p (u d) -> p u d", u=U)
        place = work[:, 2048:2048 + U * P].rearrange("p (u n) -> p u n", u=U)
        pairwin = work[0:1, 5632:5632 + NP].bitcast(i32)
        RT = NT * NX
        score = tables[:, 0:RT].rearrange("p (n e) -> p n e", e=NX)
        eq = tables[:, RT:2 * RT].rearrange("p (n e) -> p n e", e=NX)
        hot1 = tables[:, 2 * RT:3 * RT].rearrange("p (n e) -> p n e", e=NX)
        hot2 = tables[:, 3 * RT:4 * RT].rearrange("p (n e) -> p n e", e=NX)
        mask = tables[:, 4 * RT:5 * RT]
        mask3 = mask.rearrange("p (n e) -> p n e", e=NX)
        rank = tables[:, 5 * RT:6 * RT].rearrange("p (n e) -> p n e", e=NX)
        total = tables[:, 6 * RT:7 * RT].rearrange("p (e n) -> p e n", e=NX)
        incl = tables[:, 7 * RT:8 * RT].rearrange("p (e n) -> p e n", e=NX)
        excl = tables[:, 8 * RT:9 * RT].rearrange("p (e n) -> p e n", e=NX)
        xs = work[:, 0:2 * D].rearrange("p (j d) -> p j d", j=2)
        xsT = work[:, 512:512 + 2 * D].rearrange("p (j k t) -> p j k t", j=2, k=KD)
        hid = work[:, 1024:1024 + 2 * H].rearrange("p (j m) -> p j m", j=2)
        act_ = work[:, 2048:2048 + 2 * H].rearrange("p (j m) -> p j m", j=2)
        actT = work[:, 3072:3072 + 2 * H].rearrange("p (j k t) -> p j k t", j=2, k=KH)
        ys = work[:, 4096:4096 + 2 * D].rearrange("p (j d) -> p j d", j=2)
        y1 = work[:, 0:G * D].rearrange("p (g d) -> p g d", g=G)
        y2 = work[:, 2048:2048 + G * D].rearrange("p (g d) -> p g d", g=G)

        ident = sb("ident", [P, P])
        ones = sb("ones", [P, P])
        below = sb("below", [P, P])
        zeros = sb("zeros", [P, D])
        far_i = acc2[:, 6144:6144 + P].bitcast(i32)
        zero_i = acc2[:, 6272:6272 + P].bitcast(i32)
        col_i = sb("col_i", [P, P], i32)
        col_f = sb("col_f", [P, P])
        pair_i = sb("pair_i", [P, CH], i32)
        pair_f = sb("pair_f", [P, CH])
        win_f = sb("win_f", [P, NT])
        edge_f = sb("edge_f", [P, NT])
        rev_f = sb("rev_f", [P, NX])
        valid = sb("valid", [P, 1])
        spare = sb("spare", [P, 2])
        eps_t = sb("eps_t", [P, 1])
        bias_b = sb("bias_b", [P, D])
        wg_sb = sb("wg_sb", [P, KD, NX])
        bg_b = sb("bg_b", [P, NX])
        last_i = sb("last_i", [P, CH], i32)
        last_f = sb("last_f", [P, CH])
        passed = acc2[:, 5120:5120 + CH * (NT - 1)].rearrange("p (c w) -> p c w", c=CH)
        first = sb("first", [P, NT - 1])
        junk = sb("junk", [P, P])
        win = sb("win", [P, CH])
        win128 = sb("win128", [P, CH])
        win_i = sb("win_i", [P, CH], i32)
        tile_f = sb("tile_f", [P, CH])
        tile_i = sb("tile_i", [P, CH], i32)
        idx_g = sb("idx_g", [P, 2, U], i32)
        idx_s = sb("idx_s", [P, TOPK, G], i32)
        stats = sb("stats", [P, G, 6])
        moments_g = sb("moments_g", [P, G, 2])
        moments = sb("moments", [P, NT, 2])
        std = sb("std", [P, G])
        rstd = sb("rstd", [P, NT])
        best = sb("best", [P, 4, NT])
        tiles_e = sb("tiles_e", [P, NX])
        tend = sb("tend", [P, NX])
        base_e = sb("base_e", [P, NX])
        slot_f = sb("slot_f", [P, TOPK, NT])
        slot_i = sb("slot_i", [P, TOPK, NT], i32)
        owner = sb("owner", [P, 2, P])
        owner_i = sb("owner_i", [P, P], i32)
        assert FT + 2 <= P

        ps = ctx.enter_context(nc.psum_tensor("ps", [P, 8, 512], f32))

        s_x = sem("x_loaded")
        s_xpad = sem("x_pad_zeroed")
        s_wlin = sem("linear_weights_loaded")
        s_small = sem("small_loaded")
        s_edges = sem("edge_rows_written")
        s_last = sem("last_destinations_loaded")
        s_cst = sem("pool_constants")
        s_vc = sem("vector_constants")
        s_passed = sem("windows_passed_marked")
        s_first = sem("windows_first_tiles")
        s_tile = sem("pair_tiles_ready")
        s_winout = sem("pair_windows_stored")
        s_winin = sem("pair_windows_loaded")
        s_stage = sem("pair_edges_gathered")
        s_stagef = sem("pair_edges_converted")
        s_tabps = sem("pair_tables_transposed")
        s_table = sem("pair_tables_ready")
        s_v = sem("vector_chain")
        s_held = sem("pool_waits_held")
        s_statsheld = sem("stats_waits_held")
        s_stats = sem("tile_stats")
        s_momg = sem("tile_moments_found")
        s_mom = sem("tile_moments_kept")
        s_std = sem("std_ready")
        s_rstd = sem("rstd_ready")
        s_xn = sem("xn_ready")
        s_xnps = sem("xn_transposed")
        s_xnT = sem("xnT_ready")
        s_lin = sem("products_ready")
        s_takenA = sem("products_taken_by_scalar")
        s_takenV = sem("products_taken_by_vector")
        s_t3 = sem("table_rows_staged")
        s_t3free = sem("table_rows_free")
        s_t3out = sem("table_rows_written")
        s_t1 = sem("second_sums_started")
        s_bias = sem("bias_added")
        s_idx = sem("gather_indices_ready")
        s_rows = [sem(f"rows_gathered_{j}") for j in range(U)]
        s_place = sem("placement_ready")
        s_pair = sem("pair_products")
        s_acc = sem("pair_accumulated")
        s_tabout = sem("hop_table_written")
        s_w = sem("expert_weights_loaded")
        s_zero = sem("expert_rows_zeroed")
        s_mask = sem("mask_ready")
        s_rank = sem("ranks_ready")
        s_route = sem("routes_ready")
        s_didx = sem("dispatch_indices_ready")
        s_disp = sem("dispatched")
        s_dispfree = sem("dispatch_rows_free")
        s_xs = [sem(f"expert_rows_loaded_{j}") for j in range(2)]
        s_xsps = sem("expert_rows_transposed")
        s_xsT = sem("expert_rowsT_ready")
        s_h = sem("hidden_products")
        s_hb = sem("hidden_biased")
        s_act = sem("activated")
        s_actps = sem("activations_transposed")
        s_actT = sem("activationsT_ready")
        s_y = sem("expert_products")
        s_yb = sem("expert_out_ready")
        s_yout = [sem(f"expert_out_written_{j}") for j in range(2)]
        s_ysfree = sem("expert_out_slots_free")
        s_yzero = sem("spare_rows_zeroed")
        s_cidx = sem("combine_indices_ready")
        s_ygat = [sem(f"expert_out_gathered_{j}") for j in range(G)]
        s_add1 = sem("first_expert_added")
        s_add2 = sem("second_expert_added")
        s_out = sem("out_written")

        PAIRS = IT * U

        def load_registers(eng, name, count, source):
            regs = [eng.alloc_register(f"{name}_{k}") for k in range(count)]
            eng.load(regs, source)
            return regs

        block = ctx.enter_context(nc.Block())

        @block.sync
        def _(sp):
            full = (NT - 1) * P
            sp.dma_start(acc0[:, 0:NT - 1, :], x[0:full, :].rearrange("(n p) d -> p n d", p=P)).then_inc(s_x, 16)
            sp.wait_ge(s_xpad, 1)
            sp.dma_start(acc0[0:TAIL, NT - 1, :], x[full:N, :]).then_inc(s_x, 16)
            for k in range(HOPS + 1):
                sp.dma_start(wlin[:, :, (HOPS - k) * D:(HOPS - k + 1) * D],
                             gnn_w[k * D:(k + 1) * D, :].rearrange("(h p) c -> p h c", p=P)).then_inc(s_wlin, 16)
            sp.dma_start(bias_b[:, :], gnn_b.rearrange("(a n) -> a n", a=1).broadcast_to([P, D])).then_inc(s_small, 16)
            sp.dma_start(bg_b[:, :], bg.rearrange("(a n) -> a n", a=1).broadcast_to([P, NX])).then_inc(s_small, 16)
            sp.dma_start(wg_sb[:, :, :], wg.rearrange("(h p) c -> p h c", p=P)).then_inc(s_small, 16)
            sp.wait_ge(s_tile, 1)
            with nc.allow_non_contiguous_dma(reason="one value of each pair"):
                sp.dma_start(pairwin_d.rearrange("(c p) -> p c", p=P), win_i[:, :]).then_inc(s_winout, 16)
            sp.wait_ge(s_cst, 1)
            ZC = 14
            zrows = xe_d.shape[0]
            zt = zrows // P
            for a in range(0, zt, ZC):
                b = min(zt, a + ZC)
                sp.dma_start(xe_d[a * P:b * P, :].rearrange("(n p) d -> p n d", p=P),
                             zeros[:, :].unsqueeze(1).broadcast_to([P, b - a, D])).then_inc(s_zero, 16)
            sp.dma_start(ye_d[FROWS:FROWS + DUMMY, :].rearrange("(n p) d -> p n d", p=P),
                         zeros[:, :].unsqueeze(1).broadcast_to([P, TOPK, D])).then_inc(s_yzero, 16)
            with sp.Fori(0, NG) as i:
                sp.wait_ge(s_t3, i * G + G)
                sp.dma_start(table_d[0].rearrange("(n p) d -> p n d", p=P)[:, ds(i * G, G), :], t3).then_inc(s_t3out, 16)
                sp.wait_ge(s_t3out, i * 16 + 16)
                sp.sem_inc(s_t3free, 1)
            sp.wait_ge(s_winout, 16)
            sp.dma_start(pairwin, pairwin_d.rearrange("(a n) -> a n", a=1)).then_inc(s_winin, 16)
            for h in range(HOPS - 1):
                sp.wait_ge(s_acc, U + (h + 1) * PAIRS)
                sp.dma_start(table_d[h + 1].rearrange("(n p) d -> p n d", p=P), accs[h]).then_inc(s_tabout, 16)
                sp.wait_ge(s_tabout, 16 * (h + 1))
                if h == 0:
                    for k in range(KD):
                        sp.dma_start(w1_sb[:, k, :].rearrange("p (e m) -> p e m", e=NX),
                                     w1[:, k * P:(k + 1) * P, :].rearrange("e p m -> p e m")).then_inc(s_w, 16)
                    sp.dma_start(b1_sb, b1.rearrange("(a e) m -> a (e m)", a=1).broadcast_to([P, NX * H])).then_inc(s_w, 16)
                else:
                    for k in range(KH):
                        sp.dma_start(w2_sb[:, k, :].rearrange("p (e m) -> p e m", e=NX),
                                     w2[:, k * P:(k + 1) * P, :].rearrange("e p m -> p e m")).then_inc(s_w, 16)
                    sp.dma_start(b2_sb, b2.rearrange("(a e) m -> a (e m)", a=1).broadcast_to([P, NX * D])).then_inc(s_w, 16)
            sp.wait_ge(s_disp, 16 * TOPK * NT)
            sp.dma_start(xs[:, 0, :], xe_d[0:P, :]).then_inc(s_xs[0], 16)
            with sp.Fori(0, FT // 2) as i:
                for j in range(2):
                    sp.wait_ge(s_xsps, i * 2 + (2 + j))
                    sp.dma_start(xs[:, (1 + j) % 2, :], xe_d[ds((i * 2 + (1 + j)) * P, P), :]).then_inc(s_xs[(1 + j) % 2], 16)
            with sp.Fori(0, NG - 1) as i:
                sp.wait_ge(s_add2, i * G + 2 * G)
                sp.dma_start(out[0:(NG - 1) * G * P, :].rearrange("(n p) d -> p n d", p=P)[:, ds(i * G, G), :],
                             acc0[:, ds(i * G, G), :]).then_inc(s_out, 16)
            sp.wait_ge(s_add2, NT + G)
            sp.dma_start(out[(NG - 1) * G * P:(NT - 1) * P, :].rearrange("(n p) d -> p n d", p=P),
                         acc0[:, (NG - 1) * G:NT - 1, :]).then_inc(s_out, 16)
            sp.dma_start(out[(NT - 1) * P:N, :], acc0[0:TAIL, NT - 1, :]).then_inc(s_out, 16)
            sp.wait_ge(s_out, 16 * (NG + 1))

        @block.gpsimd
        def _(pool):
            def hold(semaphore, value):
                pool.wait_ge(semaphore, value)
                pool.sem_inc(s_held, 1)

            pool.memset(zeros[:, :], 0.0).then_inc(s_cst, 1)
            pool.memset(zero_i, 0).then_inc(s_cst, 1)
            pool.iota(far_i, pattern=[[0, P]], base=int(FAR), channel_multiplier=0).then_inc(s_cst, 1)
            pool.iota(col_i[:, :], pattern=[[1, P]], base=0, channel_multiplier=0).then_inc(s_cst, 1)
            pool.iota(pair_i[:, :], pattern=[[P, CH]], base=0, channel_multiplier=1).then_inc(s_cst, 1)
            pool.memset(ones[:, :], 1.0).then_inc(s_cst, 1)
            pool.memset(ident[:, :], 0.0).then_inc(s_cst, 1)
            pool.memset(eps_t[:, :], EPS).then_inc(s_cst, 1)
            pool.wait_ge(s_cst, 8)
            pool.affine_select(out=ident[:, :], in_=ident[:, :], compare_op=ALU.not_equal, fill=1.0,
                               base=0, pattern=[[-1, P]], channel_multiplier=1).then_inc(s_cst, 1)
            pool.affine_select(out=below[:, :], in_=ones[:, :], compare_op=ALU.is_gt, fill=0.0,
                               base=0, pattern=[[1, P]], channel_multiplier=-1).then_inc(s_cst, 1)
            pool.wait_ge(s_tile, 1)
            pool.wait_ge(s_edges, 16 * EDGE_DMAS)
            for c in range(CH):
                pool.indirect_dma_start(out=stage[:, c, :], out_offset=None, in_=edges_d[:, :],
                                        in_offset=bass.IndirectOffsetOnAxis(ap=tile_i[:, c:c + 1], axis=0)).then_inc(s_stage, 16)
            for h in range(HOPS):
                if h == 0:
                    pool.wait_ge(s_table, 3 * CH)
                    pool.wait_ge(s_t3out, 16 * NG)
                else:
                    pool.wait_ge(s_tabout, 16 * h)
                with pool.Fori(0, IT // 2) as i:
                    for b in range(2):
                        for j in range(U):
                            if j % 2 == 0:
                                hold(s_pair, i * (2 * U) + (h * PAIRS + b * U + j + 2))
                            if j == 0:
                                pool.tensor_copy(idx_g[:, b, :], src_t[:, ds(i * (2 * U) + b * U, U)]).then_inc(s_idx, 1)
                                hold(s_idx, i * 2 + (h * IT + b + 1))
                            pool.indirect_dma_start(out=rows[:, j, :], out_offset=None, in_=table_d[h][:, :],
                                                    in_offset=bass.IndirectOffsetOnAxis(ap=idx_g[:, b, j:j + 1], axis=0)).then_inc(s_rows[j], 16)
            pool.wait_ge(s_zero, 16 * ZERO_DMAS)
            with pool.Fori(0, NG) as i:
                hold(s_didx, i + 1)
                for j in range(G):
                    hold(s_xn, i * G + (2 * NT + j + 1))
                    for k in range(TOPK):
                        pool.indirect_dma_start(out=xe_d[:, :],
                                                out_offset=bass.IndirectOffsetOnAxis(ap=idx_s[:, k, j:j + 1], axis=0),
                                                in_=xn[:, j, :], in_offset=None).then_inc(s_disp, 16)
                pool.wait_ge(s_disp, i * (16 * TOPK * G) + 16 * TOPK * G)
                pool.sem_inc(s_dispfree, 1)
            pool.wait_ge(s_yb, 3)
            pool.dma_start(ye_d[0:P, :], ys[:, 0, :]).then_inc(s_yout[0], 16)
            pool.wait_ge(s_yb, 4)
            pool.dma_start(ye_d[P:2 * P, :], ys[:, 1, :]).then_inc(s_yout[1], 16)
            pool.wait_ge(s_yout[0], 16)
            pool.sem_inc(s_ysfree, 1)
            with pool.Fori(0, (FT - 2) // 2) as i:
                for j in range(2):
                    pool.wait_ge(s_yb, i * 2 + (5 + j))
                    pool.dma_start(ye_d[ds((i * 2 + (2 + j)) * P, P), :], ys[:, j, :]).then_inc(s_yout[j], 16)
                    pool.wait_ge(s_yout[(1 + j) % 2], i * 16 + (16 + 16 * j))
                    pool.sem_inc(s_ysfree, 1)
            for j in range(2):
                pool.wait_ge(s_yout[j], 16 * (FT // 2))
            pool.wait_ge(s_yzero, 16)
            with pool.Fori(0, NG) as i:
                pool.wait_ge(s_add2, i * G + G)
                pool.tensor_copy(idx_s[:, :, :], slot_i[:, :, ds(i * G, G)]).then_inc(s_cidx, 1)
                hold(s_cidx, i + 1)
                for j in range(G):
                    for k, y in enumerate((y1, y2)):
                        pool.indirect_dma_start(out=y[:, j, :], out_offset=None, in_=ye_d[:, :],
                                                in_offset=bass.IndirectOffsetOnAxis(ap=idx_s[:, k, j:j + 1], axis=0)).then_inc(s_ygat[j], 16)

        @block.scalar
        def _(act):
            flat = EFULL * P
            for k, a in enumerate((src, dst, edge_weight.bitcast(i32))):
                act.dma_start(edges_d[0:EFULL, k * P:(k + 1) * P], a[0:flat].rearrange("(n e) -> n e", e=P)).then_inc(s_edges, 16)
                act.dma_start(edges_d[EFULL:EFULL + 1, k * P:k * P + EREST], a[flat:E].rearrange("(n e) -> n e", n=1)).then_inc(s_edges, 16)
            act.wait_ge(s_cst, 3)
            for k in range(3):
                pad = far_i if k == 1 else zero_i
                act.dma_start(edges_d[EFULL:EFULL + 1, k * P + EREST:(k + 1) * P], pad[0:1, 0:P - EREST]).then_inc(s_edges, 16)
                act.dma_start(edges_d[EFULL + 1:NP, k * P:(k + 1) * P], pad[0:NP - EFULL - 1, :]).then_inc(s_edges, 16)
            act.wait_ge(s_edges, 16 * EDGE_DMAS)
            with nc.allow_non_contiguous_dma(reason="the last destination of each tile"):
                act.dma_start(last_i[:, :], edges_d[:, 2 * P - 1:2 * P].rearrange("(c p) a -> p (c a)", p=P)).then_inc(s_last, 16)
            for c in range(CH):
                act.wait_ge(s_tabps, 3 * c + 3)
                for k, t in enumerate((src_t, rel_t, wgt_t)):
                    act.activation(t[:, c * P:(c + 1) * P], ps[:, c % 2, k * P:(k + 1) * P], ACT.Copy).then_inc(s_table, 1)
            act.sem_inc(s_xnT, G)
            act.sem_inc(s_takenA, 1)
            act.sem_inc(s_t3free, 1)

            def xnT_copies(i, first_tile, after):
                act.wait_ge(s_mom, i + (first_tile // G + 1))
                act.activation(std[:, :], moments[:, ds(i * G, G), 1], ACT.Sqrt, bias=eps_t[:, :]).then_inc(s_std, 1)
                for j in range(G + 1):
                    if j >= 2 and after is not None:
                        after(i, j - 2)
                    if j == G:
                        break
                    act.wait_ge(s_xnps, i * G + (first_tile + G + j + 1))
                    act.wait_ge(s_lin, i * G + (first_tile + j + 1))
                    act.activation(xnT[:, j, :, :], ps[:, j % 4, 0:D].rearrange("p (k t) -> p k t", k=KD),
                                   ACT.Copy).then_inc(s_xnT, 1)

                if after is not None:
                    after(i, G - 1)

            def take(i, j):
                act.wait_ge(s_lin, i * G + (G + j + 1))
                if j == 0:
                    act.wait_ge(s_t3free, i + 1)
                act.activation(t3[:, j, :], ps[:, 4 + 2 * (j % 2), 0:D], ACT.Copy).then_inc(s_t3, 1)
                act.activation(accs[0][:, ds(i * G + j, 1), :].squeeze(1), ps[:, 4 + 2 * (j % 2), D:2 * D], ACT.Copy).then_inc(s_takenA, 1)

            with act.Fori(0, NG) as i:
                xnT_copies(i, 0, take)
            with act.Fori(0, NG) as i:
                xnT_copies(i, NT, None)
            act.sem_inc(s_xsT, 2)
            act.sem_inc(s_act, 2)
            act.sem_inc(s_actT, 2)

            def copy_xT(s, j):
                act.wait_ge(s_xsps, s + 3)
                act.wait_ge(s_h, s + 1)
                act.activation(xsT[:, j, :, :], ps[:, j, 0:D].rearrange("p (k t) -> p k t", k=KD), ACT.Copy).then_inc(s_xsT, 1)

            def gelu(s, j):
                act.wait_ge(s_hb, s + 3)
                act.wait_ge(s_actps, s + 1)
                act.activation(act_[:, j, :], hid[:, j, :], ACT.Gelu).then_inc(s_act, 1)

            def copy_actT(s, j):
                act.wait_ge(s_actps, s + 3)
                act.wait_ge(s_y, s + 1)
                act.activation(actT[:, j, :, :], ps[:, 4 + j, :].rearrange("p (k t) -> p k t", k=KH), ACT.Copy).then_inc(s_actT, 1)

            copy_xT(0, 0)
            copy_xT(1, 1)
            gelu(0, 0)
            with act.Fori(0, (FT - 2) // 2) as i:
                for j in range(2):
                    s = i * 2 + (1 + j)
                    copy_xT(s + 1, j)
                    copy_actT(s - 1, j)
                    gelu(s, (1 + j) % 2)
            s = FT - 1
            copy_xT(s + 1, (s + 1) % 2)
            copy_actT(s - 1, (s - 1) % 2)
            gelu(s, s % 2)
            copy_actT(s, s % 2)

        @block.vector
        def _(dve):
            chained = [0]

            def chain(ins):
                chained[0] += 1
                ins.then_inc(s_v, 1)
                dve.wait_ge(s_v, chained[0])

            dve.memset(acc0[:, NT - 1, :], 0.0).then_inc(s_xpad, 1)
            dve.wait_ge(s_cst, 10)
            dve.tensor_copy(col_f[:, :], col_i[:, :]).then_inc(s_vc, 1)
            dve.tensor_copy(pair_f[:, :], pair_i[:, :]).then_inc(s_vc, 1)
            dve.wait_ge(s_vc, 2)
            dve.tensor_scalar(win_f[:, :], col_f[:, 0:NT], 1.0, None, ALU.add).then_inc(s_vc, 1)
            dve.tensor_scalar(edge_f[:, :], col_f[:, 0:NT], float(P), float(P), ALU.mult, ALU.add).then_inc(s_vc, 1)
            dve.tensor_scalar(rev_f[:, :], col_f[:, 0:NX], -1.0, float(NX), ALU.mult, ALU.add).then_inc(s_vc, 1)
            dve.tensor_scalar(valid[:, :], pair_f[:, 0:1], float(TAIL), None, ALU.is_lt).then_inc(s_vc, 1)
            dve.wait_ge(s_vc, 6)
            for k in range(TOPK):
                chain(dve.tensor_scalar(spare[:, k:k + 1], pair_f[:, 0:1], float(FROWS + k * P), None, ALU.add))
            dve.wait_ge(s_last, 16)
            chain(dve.tensor_copy(last_f[:, :], last_i[:, :]))
            for c in range(CH):
                dve.tensor_scalar(passed[:, c, :], edge_f[:, 0:NT - 1], last_f[:, c:c + 1], None, ALU.is_gt).then_inc(s_passed, 1)
            dve.wait_ge(s_first, 1)
            chain(dve.tensor_tensor(first[:, :], ps[:, 0, 0:NT - 1], win_f[:, 0:NT - 1], ALU.add))
            for c in range(CH):
                chain(dve.tensor_scalar(junk[:, 0:NT - 1], first[:, :], pair_f[:, c:c + 1], None, ALU.is_le, ALU.add,
                                        accum_out=win[:, c:c + 1]))
            chain(dve.tensor_copy(win_i[:, :], win[:, :]))
            chain(dve.tensor_scalar(win128[:, :], win[:, :], float(P), None, ALU.mult))
            chain(dve.tensor_tensor(tile_f[:, :], pair_f[:, :], win[:, :], ALU.subtract))
            dve.tensor_copy(tile_i[:, :], tile_f[:, :]).then_inc(s_tile, 1)
            dve.wait_ge(s_stage, 16 * CH)
            for c in range(CH):
                dve.tensor_copy(stagef[:, c, 0:P], stage[:, c, 0:P]).then_inc(s_stagef, 1)
                dve.tensor_scalar(stagef[:, c, P:2 * P], stage[:, c, P:2 * P], win128[:, c:c + 1], None,
                                  ALU.subtract).then_inc(s_stagef, 1)

            dve.sem_inc(s_takenV, 1)

            def norm(i, first_tile):
                for j in range(G):
                    dve.bn_stats(stats[:, j, :], acc0[:, ds(i * G + j, 1), :].squeeze(1)).then_inc(s_stats, 1)
                dve.wait_ge(s_stats, i * G + (first_tile + G))
                dve.sem_inc(s_statsheld, 1)
                for j in range(G):
                    dve.bn_aggr(moments_g[:, j, :], stats[:, j, :]).then_inc(s_momg, 1)
                dve.wait_ge(s_momg, i * G + (first_tile + G))
                dve.tensor_copy(moments[:, ds(i * G, G), :], moments_g[:, :, :]).then_inc(s_mom, 1)
                dve.wait_ge(s_mom, i + (first_tile // G + 1))
                dve.wait_ge(s_std, i + (first_tile // G + 1))
                dve.reciprocal(rstd[:, ds(i * G, G)], std[:, :]).then_inc(s_rstd, 1)
                dve.wait_ge(s_rstd, i + (first_tile // G + 1))

            def centre(i, j):
                dve.tensor_scalar(xn[:, j, :], acc0[:, ds(i * G + j, 1), :].squeeze(1), moments[:, ds(i * G + j, 1), 0],
                                  rstd[:, ds(i * G + j, 1)], ALU.subtract, ALU.mult).then_inc(s_xn, 1)

            dve.wait_ge(s_x, 32)
            dve.wait_ge(s_small, 48)
            dve.wait_ge(s_table, 3 * CH)
            with dve.Fori(0, NG) as i:
                norm(i, 0)
                for j in range(G):
                    dve.wait_ge(s_xnps, i * G + (j + 1))
                    centre(i, j)
                dve.wait_ge(s_xn, i * G + G)
                for j in range(G):
                    node = acc0[:, ds(i * G + j, 1), :].squeeze(1)
                    dve.tensor_tensor(node, node, bias_b[:, :], ALU.add).then_inc(s_bias, 1)
                for j in range(G):
                    node = acc0[:, ds(i * G + j, 1), :].squeeze(1)
                    dve.wait_ge(s_lin, i * G + (G + j + 1))
                    dve.wait_ge(s_bias, i * G + (j + 1))
                    dve.tensor_copy(accs[1][:, ds(i * G + j, 1), :].squeeze(1), ps[:, 5 + 2 * (j % 2), 0:D]).then_inc(s_t1, 1)
                    dve.tensor_tensor(node, node, ps[:, 5 + 2 * (j % 2), D:2 * D], ALU.add).then_inc(s_takenV, 1)

            dve.wait_ge(s_winin, 16)
            dve.wait_ge(s_takenA, 1 + NT)
            dve.wait_ge(s_takenV, 1 + NT)
            dve.wait_ge(s_t1, NT)
            dve.sem_inc(s_acc, U)
            for h in range(HOPS):
                with dve.Fori(0, IT) as i:
                    regs = load_registers(dve, f"window_{h}", U, pairwin[0:1, ds(i * U, U)])
                    wins = [dve.snap(r, min_val=0, max_val=NT - 1) for r in regs]
                    for j in range(U):
                        dve.wait_ge(s_pair, i * U + (h * PAIRS + j + 1))
                        dve.tensor_scalar(place[:, j, :], col_f[:, :], rel_t[:, ds(i * U + j, 1)], wgt_t[:, ds(i * U + j, 1)],
                                          ALU.is_equal, ALU.mult).then_inc(s_place, 1)
                    for j in range(U):
                        dve.wait_ge(s_pair, i * U + (h * PAIRS + U + j + 1))
                        dve.wait_ge(s_acc, i * U + (h * PAIRS + U + j))
                        window = accs[h][:, ds(wins[j], 1), :].squeeze(1)
                        dve.tensor_tensor(window, window, ps[:, j, 0:D], ALU.add).then_inc(s_acc, 1)

            dve.wait_ge(s_acc, U + HOPS * PAIRS)
            with dve.Fori(0, NG) as i:
                norm(i, NT)
                for j in range(G):
                    dve.wait_ge(s_xnps, i * G + (NT + j + 1))
                    centre(i, j)
                for j in range(G):
                    dve.wait_ge(s_lin, i * G + (NT + G + j + 1))
                    dve.tensor_tensor(score[:, ds(i * G + j, 1), :].squeeze(1), ps[:, 4 + 2 * (j % 2), 0:NX], bg_b[:, :],
                                      ALU.add).then_inc(s_takenV, 1)
            dve.wait_ge(s_takenV, 1 + 2 * NT)
            rev3 = rev_f[:, :].unsqueeze(1).broadcast_to([P, NT, NX])

            def wide(a):
                return a.unsqueeze(2).broadcast_to([P, NT, NX])

            for k, hot in enumerate((hot1, hot2)):
                chain(dve.tensor_reduce(best[:, 2 * k, :], score, AX.X, ALU.max))
                chain(dve.tensor_tensor(eq, score, wide(best[:, 2 * k, :]), ALU.is_equal))
                chain(dve.tensor_tensor(eq, eq, rev3, ALU.mult))
                chain(dve.tensor_reduce(best[:, 2 * k + 1, :], eq, AX.X, ALU.max))
                chain(dve.tensor_tensor(hot, rev3, wide(best[:, 2 * k + 1, :]), ALU.is_equal))
                if k == 0:
                    chain(dve.scalar_tensor_tensor(out=score, in0=hot, scalar=-3.0e38, in1=score, op0=ALU.mult, op1=ALU.add))
            chain(dve.tensor_tensor(mask3, hot1, hot2, ALU.add))
            dve.tensor_scalar(mask3[:, NT - 1, :], mask3[:, NT - 1, :], valid[:, 0:1], None, ALU.mult).then_inc(s_mask, 1)
            dve.wait_ge(s_rank, 2)
            chain(dve.tensor_copy(rank, ps[:, 0, 0:RT].rearrange("p (n e) -> p n e", e=NX)))
            chain(dve.tensor_copy(total, ps[:, 1, 0:RT].rearrange("p (n e) -> p e n", e=NX)))
            for e in range(NX):
                chain(dve.tensor_tensor_scan(incl[:, e, :], ones[:, 0:NT], total[:, e, :], 0.0, ALU.mult, ALU.add))
            chain(dve.tensor_tensor(excl, incl, total, ALU.subtract))
            for e in range(NX):
                chain(dve.tensor_scalar(junk[:, 0:NT], edge_f[:, :], float(-P), incl[:, e, NT - 1:NT], ALU.add, ALU.is_lt))
                chain(dve.tensor_reduce(tiles_e[:, e:e + 1], junk[:, 0:NT], AX.X, ALU.add))
            chain(dve.tensor_tensor_scan(tend[:, :], ones[:, 0:NX], tiles_e[:, :], 0.0, ALU.mult, ALU.add))
            chain(dve.tensor_tensor(base_e[:, :], tend[:, :], tiles_e[:, :], ALU.subtract))
            chain(dve.tensor_scalar(base_e[:, :], base_e[:, :], float(P), None, ALU.mult))
            chain(dve.tensor_tensor(rank, rank, excl.rearrange("p e n -> p n e"), ALU.add))
            chain(dve.tensor_tensor(rank, rank, base_e[:, :].unsqueeze(1).broadcast_to([P, NT, NX]), ALU.add))
            for k, hot in enumerate((hot1, hot2)):
                chain(dve.tensor_tensor(eq, hot, rank, ALU.mult))
                chain(dve.tensor_reduce(slot_f[:, k, :], eq, AX.X, ALU.add))
                last = slot_f[:, k, NT - 1:NT]
                chain(dve.tensor_scalar(last, last, spare[:, k:k + 1], valid[:, 0:1], ALU.subtract, ALU.mult))
                chain(dve.tensor_scalar(last, last, spare[:, k:k + 1], None, ALU.add))
            chain(dve.tensor_copy(slot_i[:, :, :], slot_f[:, :, :]))
            chain(dve.memset(owner[:, 1, :], 0.0))
            for e in range(NX - 1):
                chain(dve.scalar_tensor_tensor(out=owner[:, e % 2, :], in0=col_f[:, :], scalar=tend[:, e:e + 1],
                                               in1=owner[:, (e + 1) % 2, :], op0=ALU.is_ge, op1=ALU.add))
            dve.tensor_copy(owner_i[:, :], owner[:, (NX - 2) % 2, :]).then_inc(s_route, 1)
            dve.sem_inc(s_dispfree, 1)
            with dve.Fori(0, NG) as i:
                dve.wait_ge(s_dispfree, i + 1)
                dve.tensor_copy(idx_s[:, :, :], slot_i[:, :, ds(i * G, G)]).then_inc(s_didx, 1)
                for j in range(G):
                    centre(i, j)
            dve.wait_ge(s_route, 1)
            dve.wait_ge(s_w, 16 * (KD + KH + 2))
            for s_ in (s_hb, s_yb, s_ysfree):
                dve.sem_inc(s_, 2)

            def bias_hidden(s, j, e):
                dve.wait_ge(s_h, s + 3)
                dve.wait_ge(s_act, s + 1)
                dve.tensor_tensor(hid[:, j, :], ps[:, 2 + j, :], b1_sb[:, ds(e * H, H)], ALU.add).then_inc(s_hb, 1)

            def bias_out(s, j, e):
                dve.wait_ge(s_y, s + 3)
                dve.wait_ge(s_ysfree, s + 1)
                dve.tensor_tensor(ys[:, j, :], ps[:, 6 + j, 0:D], b2_sb[:, ds(e * D, D)], ALU.add).then_inc(s_yb, 1)

            def experts(s, count, name):
                regs = load_registers(dve, name, count, owner_i[0:1, ds(s, count)])
                return [dve.snap(r, min_val=0, max_val=NX - 1) for r in regs]

            e01 = experts(0, 2, "expert_first")
            bias_hidden(0, 0, e01[0])
            bias_hidden(1, 1, e01[1])
            with dve.Fori(0, (FT - 2) // 2) as i:
                es = experts(i * 2, 4, "expert_step")
                for j in range(2):
                    s = i * 2 + (2 + j)
                    bias_hidden(s, j, es[2 + j])
                    bias_out(s - 2, j, es[j])
            el = experts(FT - 2, 2, "expert_last")
            bias_out(FT - 2, 0, el[0])
            bias_out(FT - 1, 1, el[1])
            dve.sem_inc(s_add2, G)
            with dve.Fori(0, NG) as i:
                for j in range(G):
                    node = acc0[:, ds(i * G + j, 1), :].squeeze(1)
                    dve.wait_ge(s_ygat[j], i * (16 * TOPK) + 16 * TOPK)
                    dve.tensor_tensor(node, node, y1[:, j, :], ALU.add).then_inc(s_add1, 1)
                for j in range(G):
                    node = acc0[:, ds(i * G + j, 1), :].squeeze(1)
                    dve.wait_ge(s_add1, i * G + (j + 1))
                    dve.tensor_tensor(node, node, y2[:, j, :], ALU.add).then_inc(s_add2, 1)

        @block.tensor
        def _(pe):
            pe.wait_ge(s_cst, 10)
            for c in range(CH):
                pe.wait_ge(s_passed, c + 1)
                last = pe.matmul(ps[:, 0, 0:NT - 1], ones[:, :], passed[:, c, :], start=(c == 0), stop=(c == CH - 1))
            last.then_inc(s_first, 1)
            pe.wait_ge(s_tile, 1)
            for c in range(CH):
                pe.wait_ge(s_stagef, 2 * c + 2)
                if c >= 2:
                    pe.wait_ge(s_table, 3 * (c - 1))
                for k in range(3):
                    a = stage[:, c, 2 * P:3 * P].bitcast(f32) if k == 2 else stagef[:, c, k * P:(k + 1) * P]
                    pe.transpose(ps[:, c % 2, k * P:(k + 1) * P], a, ident[:, :]).then_inc(s_tabps, 1)
            pe.wait_ge(s_table, 3 * CH)
            pe.sem_inc(s_xnps, G)
            pe.sem_inc(s_lin, G)

            def turn_nodes(i, first_tile, j):
                if j < G:
                    pe.wait_ge(s_xn, i * G + (first_tile + j + 1))
                    pe.wait_ge(s_xnT, i * G + (first_tile + G - 2 + j))
                    for k in range(KD):
                        last = pe.transpose(ps[:, j % 4, k * P:(k + 1) * P],
                                            xn[:, j, k * P:(k + 1) * P], ident[:, :])
                    last.then_inc(s_xnps, 1)

            pe.wait_ge(s_wlin, 16 * (HOPS + 1))
            with pe.Fori(0, NG) as i:
                turn_nodes(i, 0, 0)
                for j in range(G):
                    turn_nodes(i, 0, j + 1)
                    pe.wait_ge(s_xnT, i * G + (G + j + 1))
                    pe.wait_ge(s_takenA, i * G + max(j, 1))
                    pe.wait_ge(s_takenV, i * G + max(j, 1))
                    for b in range(2):
                        for k in range(KD):
                            last = pe.matmul(ps[:, 4 + 2 * (j % 2) + b, :], xnT[:, j, k, :], wlin[:, k, b * 2 * D:(b + 1) * 2 * D],
                                             start=(k == 0), stop=(k == KD - 1))
                    last.then_inc(s_lin, 1)
            pe.wait_ge(s_takenA, 1 + NT)
            pe.wait_ge(s_takenV, 1 + NT)
            pe.sem_inc(s_pair, U)
            for h in range(HOPS):
                with pe.Fori(0, IT) as i:
                    for j in range(U):
                        pe.wait_ge(s_rows[j], i * 16 + (h * IT * 16 + 16))
                        pe.wait_ge(s_place, i * U + (h * PAIRS + j + 1))
                        pe.wait_ge(s_acc, i * U + (h * PAIRS + j + 1))
                        pe.matmul(ps[:, j, 0:D], place[:, j, :], rows[:, j, :], start=True, stop=True).then_inc(s_pair, 1)
            with pe.Fori(0, NG) as i:
                turn_nodes(i, NT, 0)
                for j in range(G):
                    turn_nodes(i, NT, j + 1)
                    pe.wait_ge(s_xnT, i * G + (NT + G + j + 1))
                    pe.wait_ge(s_takenV, i * G + (NT + max(j, 1)))
                    for k in range(KD):
                        last = pe.matmul(ps[:, 4 + 2 * (j % 2), 0:NX], xnT[:, j, k, :], wg_sb[:, k, :],
                                         start=(k == 0), stop=(k == KD - 1))
                    last.then_inc(s_lin, 1)
            pe.wait_ge(s_mask, 1)
            pe.matmul(ps[:, 0, 0:RT], below[:, :], mask, start=True, stop=True).then_inc(s_rank, 1)
            pe.matmul(ps[:, 1, 0:RT], ones[:, :], mask, start=True, stop=True).then_inc(s_rank, 1)
            pe.wait_ge(s_route, 1)
            pe.wait_ge(s_w, 16 * (KD + KH + 2))
            for s_ in (s_xsps, s_h, s_actps, s_y):
                pe.sem_inc(s_, 2)

            def turn_x(s, j, loads):
                pe.wait_ge(s_xs[j], loads)
                pe.wait_ge(s_xsT, s + 1)
                for k in range(KD):
                    last = pe.transpose(ps[:, j, k * P:(k + 1) * P], xs[:, j, k * P:(k + 1) * P], ident[:, :])
                last.then_inc(s_xsps, 1)

            def hidden(s, j, e):
                pe.wait_ge(s_xsT, s + 3)
                pe.wait_ge(s_hb, s + 1)
                for k in range(KD):
                    last = pe.matmul(ps[:, 2 + j, :], xsT[:, j, k, :], w1_sb[:, k, ds(e * H, H)], start=(k == 0), stop=(k == KD - 1))
                last.then_inc(s_h, 1)

            def turn_act(s, j):
                pe.wait_ge(s_act, s + 3)
                pe.wait_ge(s_actT, s + 1)
                for k in range(KH):
                    last = pe.transpose(ps[:, 4 + j, k * P:(k + 1) * P], act_[:, j, k * P:(k + 1) * P], ident[:, :])
                last.then_inc(s_actps, 1)

            def down(s, j, e):
                pe.wait_ge(s_actT, s + 3)
                pe.wait_ge(s_yb, s + 1)
                for k in range(KH):
                    last = pe.matmul(ps[:, 6 + j, 0:D], actT[:, j, k, :], w2_sb[:, k, ds(e * D, D)], start=(k == 0), stop=(k == KH - 1))
                last.then_inc(s_y, 1)

            def experts(s, count, name):
                regs = load_registers(pe, name, count, owner_i[0:1, ds(s, count)])
                return [pe.snap(r, min_val=0, max_val=NX - 1) for r in regs]

            e01 = experts(0, 2, "expert_first")
            turn_x(0, 0, 16)
            turn_x(1, 1, 16)
            hidden(0, 0, e01[0])
            turn_x(2, 0, 32)
            hidden(1, 1, e01[1])
            turn_act(0, 0)
            with pe.Fori(0, (FT - 2) // 2) as i:
                es = experts(i * 2, 4, "expert_step")
                for j in range(2):
                    s = i * 2 + (2 + j)
                    turn_x(s + 1, (1 + j) % 2, i * 16 + (32 + 16 * j))
                    hidden(s, j, es[2 + j])
                    turn_act(s - 1, (1 + j) % 2)
                    down(s - 2, j, es[j])
            el = experts(FT - 2, 2, "expert_last")
            turn_act(FT - 1, 1)
            down(FT - 2, 0, el[0])
            down(FT - 1, 1, el[1])


EDGE_DMAS = 12
ZERO_DMAS = 8

_INS = ['x', 'src', 'dst', 'edge_weight', 'L0_gnn_shared_weight', 'L0_gnn_output_bias', 'L0_ffn_Wg', 'L0_ffn_bg',
        'L0_ffn_W1', 'L0_ffn_b1', 'L0_ffn_W2', 'L0_ffn_b2']
_OUTS = [((6250, 256), 'float32')]


def kernel(**inputs):
    import numpy as _np
    import concourse.bacc as _bacc
    from concourse import mybir as _mybir
    from concourse.bass_utils import run_bass_kernel_spmd as _run

    nc = _bacc.Bacc("TRN2", target_bir_lowering=False, num_devices=1)
    arrays, args = {}, []
    for name in _INS:
        a = _np.ascontiguousarray(inputs[name])
        arrays[f"in_{name}_dram"] = a
        args.append(nc.dram_tensor(f"in_{name}_dram", a.shape, _mybir.dt.from_np(a.dtype), kind="ExternalInput").ap())
    for i, (shape, dtype) in enumerate(_OUTS):
        dt = _mybir.dt.from_np(_np.dtype(dtype))
        args.append(nc.dram_tensor(f"out_{i}_dram", shape, dt, kind="ExternalOutput").ap())
    gnn_ffn_kernel(nc, *args)
    r = _run(nc, [arrays], core_ids=[0])
    return r.results[0]["out_0_dram"]
```
